# Optimizing a Trainium2 kernel written in Bass

```python
import numpy as np
import jax
import jax.numpy as jnp

def _softmax(x, axis=-1):
    return jax.nn.softmax(x, axis=axis)
def _gelu(x):
    return jax.nn.gelu(x, approximate=True)
def _silu(x):
    return jax.nn.silu(x)
def _sigmoid(x):
    return jax.nn.sigmoid(x)
def _layernorm(x, axis=-1, eps=1e-5):
    m = jnp.mean(x, axis=axis, keepdims=True)
    v = jnp.var(x, axis=axis, keepdims=True)
    return (x - m) / jnp.sqrt(v + eps)
def _scatter_add(tgt, idx, src, axis=0):
    return tgt.at[idx].add(src)
def _segment_sum(src, seg, n):
    return jax.ops.segment_sum(src, seg, n)

kernel_name = 'mk_adj_resnorm_d1_adj_256_44df92'

def setup_inputs(seed: int = 0):
    np.random.seed(seed)
    _w = jnp.asarray
    def _rec_inputs():
        import jax
        import jax.numpy as jnp
        _gk = jax.random.key(seed)
        x = -0.0005146 + 1 * jax.random.normal(jax.random.fold_in(_gk, 1), (8, 2048, 256), jnp.float32)
        _w = (1.0 + jnp.arange(2048, dtype=jnp.float32)) ** -0.5
        _w = _w / _w.mean()
        _pij = jnp.clip(0.015625 * _w[:, None] * _w[None, :], 0.0, 1.0)
        _a = jax.random.uniform(jax.random.fold_in(_gk, 2), (8, 2048, 2048)) < _pij
        adj = _a.astype(jnp.int32)
        return x, adj
    x, adj = _rec_inputs()
    def _L0_gnn_setup():
        import jax, jax.numpy as jnp
        import numpy as np
        B, N, C, OUT, S = (4, 2048, 256, 256, 25)
        DENSITY = 0.008
        key = jax.random.key(seed)
        kA, kX, kW = jax.random.split(key, 3)
        A = jax.random.bernoulli(kA, DENSITY, (B, N, N)).astype(jnp.int32)
        X = jax.random.normal(kX, (B, N, C), dtype=jnp.float32)
        W = jax.random.normal(kW, (2 * C, OUT), dtype=jnp.float32) * np.float32(1.0 / np.sqrt(2 * C))
        b = jnp.zeros((OUT,), dtype=jnp.float32)
        return {'A': A, 'X': X, 'W': W, 'b': b}
    _L0_gnn_all = _L0_gnn_setup()
    _L0_gnn_in = {k: v for k, v in _L0_gnn_all.items() if k in ('W', 'b', )}
    del _L0_gnn_all

    return {
        "x": x,
        "adj": adj,
        "L0_gnn_W": _L0_gnn_in["W"],
        "L0_gnn_b": _L0_gnn_in["b"],
    }

def reference(x, adj, L0_gnn_W, L0_gnn_b):
    import jax
    import jax.numpy as jnp
    def _L0_gnn_ref(A, X, W, b):
        import jax, jax.numpy as jnp
        import numpy as np
        B, N, C, OUT, S = (4, 2048, 256, 256, 25)
        DENSITY = 0.008
        mask = A != 0
        neg_inf = jnp.float32(-jnp.inf)
        pri = -jnp.arange(N, dtype=jnp.float32)
        scores = jnp.where(mask, pri, neg_inf)
        vals, idx = jax.lax.top_k(scores, S)
        valid = vals > neg_inf
        feats = jax.vmap(lambda x, i: x[i])(X, idx)
        feats = jnp.where(valid[..., None], feats, neg_inf)
        agg = feats.max(axis=2)
        degree = mask.sum(axis=-1)
        agg = jnp.where((degree <= S)[..., None], jnp.maximum(agg, 0.0), agg)
        h = jnp.concatenate([X, agg], axis=-1)
        out = jax.nn.relu(jnp.einsum('bnf,fo->bno', h, W) + b)
        return out

    x = _layernorm(x + _L0_gnn_ref(adj, x, L0_gnn_W, L0_gnn_b), axis=-1)
    return x


_drawn_inputs = setup_inputs


def setup_inputs(seed=0):
    import zlib

    import numpy as np

    out = dict(_drawn_inputs(seed))
    spreads = {'L0_gnn_b': (0.0, 0.1)}
    factors = {}
    for name, (base, spread) in spreads.items():
        noise = np.random.default_rng([zlib.crc32(name.encode()), seed]).standard_normal(out[name].shape)
        drawn = base * np.exp(spread * noise) if base else spread * noise
        out[name] = jnp.asarray(drawn.astype(out[name].dtype))
    for name, factor in factors.items():
        out[name] = (out[name] * factor).astype(out[name].dtype)
    return out
```

```python
from contextlib import ExitStack

import concourse.bass as bass
from concourse import mybir

P = 128
S = 25
WORD = 8
TOP = 32
WORDS_KEPT = S + 1
CAND = WORDS_KEPT * WORD
EPS = 1e-5
BIG = 3.4028234663852886e38

ALU = mybir.AluOpType
ACT = mybir.ActivationFunctionType
AX = mybir.AxisListType
BF16 = mybir.dt.bfloat16
F32 = mybir.dt.float32
I32 = mybir.dt.int32


def build(nc, x, adj, w, bias, out):
    B, N, C = x.shape
    OUT = w.shape[1]
    TILES = B * N // P
    PER_GRAPH = N // P
    CHUNKS = N // P
    NW = N // WORD
    WPC = P // WORD
    CT = C // P
    KT = w.shape[0] // P
    assert TILES % 2 == 0 and PER_GRAPH % 2 == 0 and KT == 2 * CT
    OFF = N + WORD

    x_rows = x.rearrange("b n c -> (b n) c")
    x_tiles = x.rearrange("b (t p) c -> (b t) p c", p=P)
    adj_tiles = adj.rearrange("b (t p) m -> (b t) p m", p=P)
    out_tiles = out.rearrange("b (t p) c -> (b t) p c", p=P)

    with ExitStack() as ctx:
        def sb(name, shape, dt):
            return ctx.enter_context(nc.sbuf_tensor(name, shape, dt))

        def ps(name, shape, dt):
            return ctx.enter_context(nc.psum_tensor(name, shape, dt))

        def sem(name):
            return ctx.enter_context(nc.semaphore(name))

        ident_b = sb("ident_b", [P, P], BF16)
        ident_f = sb("ident_f", [P, P], F32)
        pack_f = sb("pack_f", [P, WPC], F32)
        pack_tmp = sb("pack_tmp", [P, WPC, WORD], F32)
        pack = sb("pack", [P, WPC], BF16)
        word_rank = sb("word_rank", [P, NW], F32)
        bit_of = sb("bit_of", [P, WORDS_KEPT, WORD], I32)
        behind = sb("behind", [P, WORDS_KEPT, WORD], F32)
        row_base = sb("row_base", [P, TILES // 2], F32)
        ones_row = sb("ones_row", [1, P], F32)
        w_sb = sb("w_sb", [P, KT, OUT], F32)
        b_row = sb("b_row", [1, OUT], F32)
        eps_col = sb("eps_col", [P, 1], F32)

        adj_sb = sb("adj_sb", [P, 2, N], I32)
        x_sb = sb("x_sb", [P, 2, C], F32)
        sign = sb("sign", [P, 2, N], BF16)
        mask_t = sb("mask_t", [P, 2, N], BF16)
        got = sb("got", [P, 2, S, C], F32)
        index = sb("index", [P, 2, TOP], I32)
        low = sb("low", [P, 2], F32)
        high = sb("high", [P, 2], F32)
        h_t = sb("h_t", [P, 2, KT * P], F32)
        y = sb("y", [P, 2, OUT], F32)
        shift = sb("shift", [P, 2], F32)
        rstd = sb("rstd", [P, 2], F32)
        std = sb("std", [P, 2], F32)
        stat = sb("stat", [P, 2, 2], F32)
        result = sb("result", [P, 2, OUT], F32)
        agg = sb("agg", [P, 2, C], F32)

        ranked = sb("ranked", [P, NW], F32)
        key = sb("key", [P, NW], F32)
        word_top = sb("word_top", [P, TOP], F32)
        word_int = sb("word_int", [P, WORDS_KEPT], I32)
        word_at = sb("word_at", [P, WORDS_KEPT], I32)
        bits_on = sb("bits_on", [P, WORDS_KEPT, WORD], I32)
        score = sb("score", [P, WORDS_KEPT, WORD], F32)
        cand = sb("cand", [P, CAND], F32)
        top = sb("top", [P, TOP], F32)
        first = sb("first", [P, 1], F32)
        fill = sb("fill", [P, S], F32)
        chosen = sb("chosen", [P, S], F32)
        agg_raw = sb("agg_raw", [P, C], F32)
        halves = sb("halves", [P, 6], F32)

        turned_ps = ps("turned_ps", [P, N], BF16)
        bits_ps = ps("bits_ps", [P, 2, 512], F32)
        ht_ps = ps("ht_ps", [P, KT * P], F32)
        layer_ps = ps("layer_ps", [P, 512], F32)

        const_pool = sem("const_pool")
        const_vec = sem("const_vec")
        weights_in = sem("weights_in")
        adj_in = [sem(f"adj_in{i}") for i in range(2)]
        x_in = [sem(f"x_in{i}") for i in range(2)]
        sign_ready = sem("sign_ready")
        turned = sem("turned")
        mask_ready = sem("mask_ready")
        bits_ready = sem("bits_ready")
        bits_used = sem("bits_used")
        index_ready = sem("index_ready")
        gathering = sem("gathering")
        gathered = [sem(f"gathered{i}") for i in range(2)]
        got_used = sem("got_used")
        agg_ready = sem("agg_ready")
        ht_ready = sem("ht_ready")
        ht_moved = sem("ht_moved")
        layer_ready = sem("layer_ready")
        y_ready = sem("y_ready")
        stat_ready = sem("stat_ready")
        std_ready = sem("std_ready")
        scale_ready = sem("scale_ready")
        result_ready = sem("result_ready")
        stored = [sem(f"stored{i}") for i in range(2)]
        vec = sem("vec")

        block = ctx.enter_context(nc.Block())
        PAIRS = TILES // 2

        @block.sync
        def _(sp):
            sp.dma_start(w_sb[:], w.rearrange("(k p) o -> p k o", p=P)).then_inc(weights_in, 16)
            sp.dma_start(b_row[:], bias.rearrange("(a o) -> a o", a=1)).then_inc(weights_in, 16)

            def load_adj(t, i):
                sp.dma_start(adj_sb[:, i, :], adj_tiles[t]).then_inc(adj_in[i], 16)

            def load_x(t, i):
                sp.dma_start(x_sb[:, i, :], x_tiles[t]).then_inc(x_in[i], 16)

            def store(t, i):
                sp.dma_start(out_tiles[t], result[:, i, :]).then_inc(stored[i], 16)

            for i in range(2):
                load_adj(i, i)
                load_x(i, i)
            with sp.Fori(0, PAIRS - 1) as j:
                for i in range(2):
                    sp.wait_ge(sign_ready, 2 * j + i + 1)
                    load_adj(2 * j + (i + 2), i)
                for i in range(2):
                    sp.wait_ge(y_ready, 2 * j + i + 1)
                    load_x(2 * j + (i + 2), i)
                    sp.wait_ge(result_ready, 2 * j + i + 1)
                    store(2 * j + i, i)
            for i in range(2):
                sp.wait_ge(result_ready, TILES - 1 + i)
                store(TILES - 2 + i, i)
            for i in range(2):
                sp.wait_ge(stored[i], 16 * PAIRS)

        CONST_POOL = 8 + WORD + 2 + WORD

        @block.gpsimd
        def _(pool):
            pool.memset(ident_b[:], 0.0).then_inc(const_pool, 1)
            pool.memset(ident_f[:], 0.0).then_inc(const_pool, 1)
            pool.memset(pack_tmp[:], 0.0).then_inc(const_pool, 1)
            pool.memset(ones_row[:], 1.0).then_inc(const_pool, 1)
            pool.memset(eps_col[:], EPS).then_inc(const_pool, 1)
            pool.iota(word_rank[:], pattern=[[-256, NW]], base=256 * NW, channel_multiplier=0,
                      allow_small_or_imprecise_dtypes=True).then_inc(const_pool, 1)
            pool.iota(behind[:], pattern=[[0, WORDS_KEPT], [-1, WORD]], base=WORD, channel_multiplier=0,
                      allow_small_or_imprecise_dtypes=True).then_inc(const_pool, 1)
            pool.iota(row_base[:].rearrange("p (b h) -> p b h", b=B), pattern=[[N, B], [0, PER_GRAPH // 2]],
                      base=OFF, channel_multiplier=0,
                      allow_small_or_imprecise_dtypes=True).then_inc(const_pool, 1)
            for c in range(WORD):
                pool.memset(bit_of[:, :, c], 1 << (WORD - 1 - c)).then_inc(const_pool, 1)
            pool.wait_ge(const_pool, 8 + WORD)
            for m in (ident_b, ident_f):
                pool.affine_select(out=m[:], in_=m[:], compare_op=ALU.not_equal, fill=1.0, base=0,
                                   pattern=[[-1, P]], channel_multiplier=1).then_inc(const_pool, 1)
            for c in range(WORD):
                pool.affine_select(out=pack_tmp[:, :, c], in_=pack_tmp[:, :, c], compare_op=ALU.not_equal,
                                   fill=float(1 << (WORD - 1 - c)), base=-c, pattern=[[-WORD, WPC]],
                                   channel_multiplier=1).then_inc(const_pool, 1)

            def gather(i):
                for k in range(S):
                    pool.indirect_dma_start(
                        out=got[:, i, k, :], out_offset=None, in_=x_rows,
                        in_offset=bass.IndirectOffsetOnAxis(ap=index[:, i, k:k + 1], axis=0),
                    ).then_inc(gathered[i], 16)

            for i in range(2):
                pool.wait_ge(index_ready, i + 1)
                gather(i)
            with pool.Fori(1, PAIRS) as j:
                for i in range(2):
                    pool.wait_ge(index_ready, 2 * j + i + 1)
                    pool.wait_ge(got_used, 2 * j + i - 1)
                    pool.sem_inc(gathering, 1)
                    gather(i)

        @block.scalar
        def _(act):
            def make_mask(j, i):
                act.wait_ge(adj_in[i], 16 * (j + 1))
                act.activation(sign[:, i, :], adj_sb[:, i, :], ACT.Sign).then_inc(sign_ready, 1)

            def move_mask(j, i):
                act.wait_ge(turned, 2 * j + i + 1)
                act.activation(mask_t[:, i, :], turned_ps[:], ACT.Square).then_inc(mask_ready, 1)

            def move_h(j, i):
                act.wait_ge(ht_ready, 2 * j + i + 1)
                act.activation(h_t[:, i, :], ht_ps[:], ACT.Copy).then_inc(ht_moved, 1)

            def take_std(j, i):
                act.wait_ge(stat_ready, 2 * j + i + 1)
                act.activation(std[:, i:i + 1], stat[:, i, 1:2], ACT.Sqrt,
                               bias=eps_col[:]).then_inc(std_ready, 1)

            def normalize(j, i, stored_before):
                act.wait_ge(scale_ready, 2 * j + i + 1)
                if stored_before:
                    act.wait_ge(stored[i], 16 * j)
                act.activation(result[:, i, :], y[:, i, :], ACT.Identity, bias=shift[:, i:i + 1],
                               scale=rstd[:, i:i + 1]).then_inc(result_ready, 1)

            act.wait_ge(const_pool, 8 + WORD)
            for i in range(2):
                make_mask(0, i)
                move_mask(0, i)
            for i in range(2):
                make_mask(1, i)
                move_mask(1, i)
                move_h(0, i)
                take_std(0, i)
                normalize(0, i, False)
            with act.Fori(1, PAIRS - 1) as j:
                for i in range(2):
                    make_mask(j + 1, i)
                    move_mask(j + 1, i)
                    move_h(j, i)
                    take_std(j, i)
                    normalize(j, i, True)
            for i in range(2):
                move_h(PAIRS - 1, i)
                take_std(PAIRS - 1, i)
                normalize(PAIRS - 1, i, True)

        @block.tensor
        def _(pe):
            def turn_mask(j, i, before):
                pe.wait_ge(sign_ready, 2 * j + i + 1)
                if before:
                    pe.wait_ge(mask_ready, 2 * j + i)
                for c in range(CHUNKS):
                    mm = pe.transpose(turned_ps[:, c * P:(c + 1) * P], sign[:, i, c * P:(c + 1) * P], ident_b[:])
                mm.then_inc(turned, 1)

            def pack_words(j, i, before):
                pe.wait_ge(mask_ready, 2 * j + i + 1)
                if before:
                    pe.wait_ge(bits_used, 2 * j + i - 1)
                for c in range(CHUNKS):
                    mm = pe.matmul(bits_ps[:, i, c * WPC:(c + 1) * WPC], mask_t[:, i, c * P:(c + 1) * P],
                                   pack[:], start=True, stop=True)
                mm.then_inc(bits_ready, 1)

            def turn_h(j, i, before):
                pe.wait_ge(x_in[i], 16 * (j + 1))
                if before:
                    pe.wait_ge(ht_moved, 2 * j + i)
                pe.wait_ge(agg_ready, 2 * j + i + 1)
                for c in range(CT):
                    pe.transpose(ht_ps[:, c * P:(c + 1) * P], x_sb[:, i, c * P:(c + 1) * P], ident_f[:])
                for c in range(CT):
                    mm = pe.transpose(ht_ps[:, (CT + c) * P:(CT + c + 1) * P], agg[:, i, c * P:(c + 1) * P],
                                      ident_f[:])
                mm.then_inc(ht_ready, 1)

            def layer(j, i, before):
                if before:
                    pe.wait_ge(y_ready, 2 * j + i)
                pe.matmul(layer_ps[:, 0:OUT], ones_row[:], b_row[:], start=True, stop=False)
                pe.wait_ge(ht_moved, 2 * j + i + 1)
                for k in range(KT):
                    mm = pe.matmul(layer_ps[:, 0:OUT], h_t[:, i, k * P:(k + 1) * P], w_sb[:, k, :],
                                   start=False, stop=(k == KT - 1))
                mm.then_inc(layer_ready, 1)

            pe.wait_ge(const_pool, CONST_POOL)
            pe.wait_ge(const_vec, 2)
            pe.wait_ge(weights_in, 32)
            for i in range(2):
                turn_mask(0, i, i > 0)
                pack_words(0, i, False)
            for i in range(2):
                turn_mask(1, i, True)
                pack_words(1, i, True)
                turn_h(0, i, i > 0)
                layer(0, i, i > 0)
            with pe.Fori(1, PAIRS - 1) as j:
                for i in range(2):
                    turn_mask(j + 1, i, True)
                    pack_words(j + 1, i, True)
                    turn_h(j, i, True)
                    layer(j, i, True)
            for i in range(2):
                turn_h(PAIRS - 1, i, True)
                layer(PAIRS - 1, i, True)

        @block.vector
        def _(dve):
            dve.wait_ge(const_pool, CONST_POOL)
            dve.tensor_reduce(pack_f[:], pack_tmp[:], AX.X, ALU.add).then_inc(const_vec, 1)
            dve.wait_ge(const_vec, 1)
            dve.tensor_copy(pack[:], pack_f[:]).then_inc(const_vec, 1)

            links = [0]

            def link(ins):
                ins.then_inc(vec, 1)
                links[0] += 1
                dve.wait_ge(vec, links[0])

            def restart():
                dve.sem_clear(vec)
                links[0] = 0

            def top_of(values, best):
                for r in range(0, TOP, 8):
                    link(dve.max(best[:, r:r + 8], values))
                    if r + 8 < TOP:
                        link(dve.match_replace(values, best[:, r:r + 8], values, 0.0))

            def find(j, i):
                dve.wait_ge(bits_ready, 2 * j + i + 1)
                link(dve.scalar_tensor_tensor(ranked[:], bits_ps[:, i, 0:NW], 0.0, word_rank[:], ALU.is_gt, ALU.mult))
                link(dve.tensor_tensor(key[:], ranked[:], bits_ps[:, i, 0:NW], ALU.add))
                dve.engine_nop().then_inc(bits_used, 1)
                top_of(key[:], word_top)
                link(dve.tensor_copy(word_int[:], word_top[:, 0:WORDS_KEPT]))
                link(dve.tensor_scalar(word_at[:], word_int[:], 8, 3, ALU.logical_shift_right,
                                       ALU.logical_shift_left))
                link(dve.tensor_tensor(bits_on[:], word_int[:, :, None].to_broadcast([P, WORDS_KEPT, WORD]),
                                       bit_of[:], ALU.bitwise_and))
                link(dve.tensor_tensor(score[:], word_at[:, :, None].to_broadcast([P, WORDS_KEPT, WORD]),
                                       behind[:], ALU.add))
                link(dve.scalar_tensor_tensor(cand[:], bits_on[:].rearrange("p a b -> p (a b)"), 0.0,
                                              score[:].rearrange("p a b -> p (a b)"), ALU.is_gt, ALU.mult))
                top_of(cand[:], top)
                dve.tensor_scalar(low[:, i:i + 1], top[:, S:S + 1], 0.0, -BIG, ALU.is_gt, ALU.mult)
                dve.tensor_scalar(high[:, i:i + 1], top[:, 0:1], 0.0, BIG, ALU.is_gt, ALU.mult)
                link(dve.tensor_scalar_max(first[:], top[:, 0:1], float(WORD + 1)))
                link(dve.tensor_scalar(fill[:], top[:, 0:S], 0.0, first[:], ALU.is_equal, ALU.mult))
                link(dve.tensor_tensor(chosen[:], fill[:], top[:, 0:S], ALU.add))
                base = row_base[:, bass.ds(j, 1)]
                dve.tensor_scalar(index[:, i, 0:S], chosen[:], -1.0, base, ALU.mult, ALU.add).then_inc(index_ready, 1)

            def reduce(j, i, before):
                dve.wait_ge(gathered[i], 16 * S * (j + 1))
                dve.tensor_reduce(agg_raw[:], got[:, i, :, :].rearrange("p k c -> p c k"), AX.X,
                                  ALU.max).then_inc(got_used, 1)
                dve.wait_ge(got_used, 2 * j + i + 1)
                if before:
                    dve.wait_ge(ht_ready, 2 * j + i - 1)
                dve.tensor_scalar(agg[:, i, :], agg_raw[:], low[:, i:i + 1], high[:, i:i + 1],
                                  ALU.max, ALU.min).then_inc(agg_ready, 1)

            def finish(j, i, before):
                dve.wait_ge(layer_ready, 2 * j + i + 1)
                if before:
                    dve.wait_ge(result_ready, 2 * j + i - 1)
                dve.scalar_tensor_tensor(y[:, i, :], layer_ps[:, 0:OUT], 0.0, x_sb[:, i, :], ALU.max,
                                         ALU.add).then_inc(y_ready, 1)
                dve.wait_ge(y_ready, 2 * j + i + 1)
                link(dve.bn_stats(halves[:], y[:, i, :]))
                dve.bn_aggr(stat[:, i, :], halves[:]).then_inc(stat_ready, 1)
                dve.wait_ge(std_ready, 2 * j + i + 1)
                link(dve.reciprocal(rstd[:, i:i + 1], std[:, i:i + 1]))
                dve.scalar_tensor_tensor(shift[:, i:i + 1], stat[:, i, 0:1], -1.0, rstd[:, i:i + 1],
                                         ALU.mult, ALU.mult).then_inc(scale_ready, 1)

            def pair(j, before):
                find(j + 1, 0)
                reduce(j, 1, before)
                finish(j, 0, before)
                find(j + 1, 1)
                reduce(j + 1, 0, True)
                finish(j, 1, before)

            find(0, 0)
            find(0, 1)
            reduce(0, 0, False)
            pair(0, False)
            restart()
            with dve.Fori(1, PAIRS - 1) as j:
                pair(j, True)
                restart()
            reduce(PAIRS - 1, 1, True)
            finish(PAIRS - 1, 0, True)
            finish(PAIRS - 1, 1, True)


_INS = ["x", "adj", "L0_gnn_W", "L0_gnn_b"]


def kernel(**inputs):
    import numpy as np
    import concourse.bacc as bacc
    from concourse.bass_utils import run_bass_kernel_spmd

    nc = bacc.Bacc("TRN2", target_bir_lowering=False, num_devices=1)
    arrays, args = {}, []
    for name in _INS:
        a = np.ascontiguousarray(inputs[name])
        arrays[f"in_{name}"] = a
        args.append(nc.dram_tensor(f"in_{name}", a.shape, mybir.dt.from_np(a.dtype), kind="ExternalInput").ap())
    out = nc.dram_tensor("out", inputs["x"].shape, F32, kind="ExternalOutput").ap()
    build(nc, *args, out)
    return run_bass_kernel_spmd(nc, [arrays], core_ids=[0]).results[0]["out"]
```

```python
from contextlib import ExitStack

import concourse.bass as bass
from concourse import mybir

P = 128
S = 25
WINDOW = (2, 3, 4, 5, 5, 6)
LOW = len(WINDOW)
FAR = S - LOW
EARLY = FAR // 2 + 1
WORD = 8
TOP = 32
WORDS_KEPT = S + 1
CAND = WORDS_KEPT * WORD
SELF = 1024.0
PARTS = 3
BANK = 512
EPS = 1e-5
BIG = 3.4028234663852886e38

ALU = mybir.AluOpType
ACT = mybir.ActivationFunctionType
AX = mybir.AxisListType
BF16 = mybir.dt.bfloat16
F16 = mybir.dt.float16
F32 = mybir.dt.float32
I32 = mybir.dt.int32


def build(nc, x, adj, w, bias, out):
    B, N, C = x.shape
    OUT = w.shape[1]
    TILES = B * N // P
    PAIRS = TILES // 2
    PER_GRAPH = N // P
    PPG = PER_GRAPH // 2
    CHUNKS = N // P
    NW = N // WORD
    WPC = P // WORD
    CT = C // P
    KT = w.shape[0] // P
    WIN = max(WINDOW)
    HOTS = sum(WINDOW)
    HOT_AT = [sum(WINDOW[:q]) for q in range(LOW)]
    OFF = N + WORD
    assert TILES % 2 == 0 and PER_GRAPH % 2 == 0 and KT == 2 * CT
    assert LOW == 6
    assert 1 < WIN and WIN * P < SELF and 4 * (WIN * P + C) <= 2 * N and N <= 2 * SELF

    x_rows = x.rearrange("b n c -> (b n) c")
    x_tiles = x.rearrange("b (t p) c -> (b t) p c", p=P)
    x_heads = x[:, 0:WIN * P, :].rearrange("b (c p) f -> b p c f", p=P)
    adj_tiles = adj.rearrange("b (t p) m -> (b t) p m", p=P)
    out_tiles = out.rearrange("b (t p) c -> (b t) p c", p=P)

    with ExitStack() as ctx:
        def sb(name, shape, dt):
            return ctx.enter_context(nc.sbuf_tensor(name, shape, dt))

        def ps(name, shape, dt):
            return ctx.enter_context(nc.psum_tensor(name, shape, dt))

        def sem(name):
            return ctx.enter_context(nc.semaphore(name))

        ident_b = sb("ident_b", [P, P], BF16)
        ident_f = sb("ident_f", [P, P], F32)
        ones_b = sb("ones_b", [P, P], BF16)
        before_b = sb("before_b", [P, P], BF16)
        pack_f = sb("pack_f", [P, WPC], F32)
        pack_tmp = sb("pack_tmp", [P, WPC, WORD], F32)
        pack = sb("pack", [P, WPC], BF16)
        word_rank = sb("word_rank", [P, NW], F32)
        bit_of = sb("bit_of", [P, WORDS_KEPT, WORD], I32)
        behind = sb("behind", [P, WORDS_KEPT, WORD], F32)
        row_base = sb("row_base", [P, PAIRS], F32)
        edge = sb("edge", [P, LOW], F32)
        ones_row = sb("ones_row", [1, P], F32)
        ones_col = sb("ones_col", [P, 1], F32)
        w_sb = sb("w_sb", [P, KT, OUT], F32)
        b_row = sb("b_row", [1, OUT], F32)
        eps_col = sb("eps_col", [P, 1], F32)

        adj_sb = sb("adj_sb", [P, 2, N], I32)
        x_sb = sb("x_sb", [P, 2, C], F32)
        sign = sb("sign", [P, 2, N], BF16)
        mask_t = sb("mask_t", [P, 2, N], BF16)
        rank = sb("rank", [P, 2, WIN * P], F16)
        hot = sb("hot", [P, 2, HOTS * P], BF16)
        got = sb("got", [P, 2, FAR + 2, C], F32)
        index = sb("index", [P, 2, FAR], I32)
        index_low = sb("index_low", [P, 2, LOW], I32)
        flag = sb("flag", [1, 2], I32)
        low = sb("low", [P, 2], F32)
        high = sb("high", [P, 2], F32)
        agg = sb("agg", [P, 2, C], F32)
        h_t = sb("h_t", [P, 2, KT * P], F32)
        y = sb("y", [P, 2, OUT], F32)
        stat = sb("stat", [P, 2, 2], F32)
        std = sb("std", [P, 2], F32)
        rstd = sb("rstd", [P, 2], F32)
        shift = sb("shift", [P, 2], F32)
        result = sb("result", [P, 2, OUT], F32)

        got_low = sb("got_low", [P, LOW, C], F32)
        x_rest = sb("x_rest", [P, WIN, C], F32)
        parts_next = sb("parts_next", [P, WIN, PARTS, C], BF16)
        parts = sb("parts", [P, WIN, PARTS, C], BF16)

        ranked = sb("ranked", [P, NW], F32)
        key = sb("key", [P, NW], F32)
        word_top = sb("word_top", [P, TOP], F32)
        word_int = sb("word_int", [P, WORDS_KEPT], I32)
        word_at = sb("word_at", [P, WORDS_KEPT], I32)
        bits_on = sb("bits_on", [P, WORDS_KEPT, WORD], I32)
        score = sb("score", [P, WORDS_KEPT, WORD], F32)
        cand = sb("cand", [P, CAND], F32)
        top = sb("top", [P, TOP], F32)
        first = sb("first", [P, 1], F32)
        spare = sb("spare", [P, FAR], F32)
        empty_low = sb("empty_low", [P, LOW], F32)
        fill = sb("fill", [P, FAR], F32)
        chosen = sb("chosen", [P, FAR], F32)
        outside = sb("outside", [P, LOW], F32)
        over = sb("over", [P, LOW], F32)
        all_max = sb("all_max", [P, C], F32)
        halves = sb("halves", [P, 6], F32)

        turned_ps = ps("turned_ps", [P, N], BF16)
        rank_ps = turned_ps[:].bitcast(F32)
        turn_ps = rank_ps[:, WIN * P:WIN * P + C]
        bits_ps = ps("bits_ps", [P, BANK], F32)
        flag_ps = bits_ps[0:1, NW:NW + LOW]
        low_ps = ps("low_ps", [P, LOW, C], F32)
        layer_ps = ps("layer_ps", [P, BANK], F32)

        const_pool = sem("const_pool")
        const_vec = sem("const_vec")
        weights_in = sem("weights_in")
        adj_in = [sem(f"adj_in{i}") for i in range(2)]
        x_in = [sem(f"x_in{i}") for i in range(2)]
        sign_ready = sem("sign_ready")
        turned = sem("turned")
        mask_ready = sem("mask_ready")
        ranks_in_ps = sem("ranks_in_ps")
        rank_ready = sem("rank_ready")
        bits_ready = sem("bits_ready")
        bits_used = sem("bits_used")
        hot_ready = sem("hot_ready")
        index_ready = sem("index_ready")
        over_ready = sem("over_ready")
        flag_in_ps = sem("flag_in_ps")
        flag_ready = sem("flag_ready")
        far_begun = sem("far_begun")
        low_begun = sem("low_begun")
        flag_known = sem("flag_known")
        flag_seen = sem("flag_seen")
        gathered = [[sem(f"gathered{i}_{part}") for part in ("early", "late")] for i in range(2)]
        low_gathered = sem("low_gathered")
        low_settled = sem("low_settled")
        got_used = sem("got_used")
        low_ready = sem("low_ready")
        agg_ready = sem("agg_ready")
        xt_ready = sem("xt_ready")
        xt_moved = sem("xt_moved")
        at_ready = sem("at_ready")
        at_moved = sem("at_moved")
        layer_ready = sem("layer_ready")
        y_ready = sem("y_ready")
        stat_ready = sem("stat_ready")
        std_ready = sem("std_ready")
        scale_ready = sem("scale_ready")
        result_ready = sem("result_ready")
        stored = [sem(f"stored{i}") for i in range(2)]
        split_in = sem("split_in")
        part_ready = sem("part_ready")
        rest_ready = sem("rest_ready")
        parts_placed = sem("parts_placed")
        vec = sem("vec")

        CONST_FILLS = 11 + WORD + LOW
        CONST_POOL = CONST_FILLS + 4 + WORD

        block = ctx.enter_context(nc.Block())

        @block.sync
        def _(sp):
            def load_adj(t, i):
                sp.dma_start(adj_sb[:, i, :], adj_tiles[t]).then_inc(adj_in[i], 16)

            def load_x(t, i):
                sp.dma_start(x_sb[:, i, :], x_tiles[t]).then_inc(x_in[i], 16)

            def load_split(g):
                sp.dma_start(x_rest[:], x_heads[g]).then_inc(split_in, 16)

            def store(t, i):
                sp.dma_start(out_tiles[t], result[:, i, :]).then_inc(stored[i], 16)

            def step(j, i, first=False, last=False):
                if not last:
                    sp.wait_ge(sign_ready, 2 * j + i + 1)
                    load_adj(2 * j + (i + 2), i)
                if not first:
                    if not (last and i == 1):
                        sp.wait_ge(y_ready, 2 * j + i)
                        load_x(2 * j + (i + 1), 1 - i)
                    sp.wait_ge(result_ready, 2 * j + i)
                    store(2 * j + (i - 1), 1 - i)

            load_adj(0, 0)
            load_adj(1, 1)
            load_split(0)
            load_x(0, 0)
            load_x(1, 1)
            sp.dma_start(w_sb[:], w.rearrange("(k p) o -> p k o", p=P)).then_inc(weights_in, 16)
            sp.dma_start(b_row[:], bias.rearrange("(a o) -> a o", a=1)).then_inc(weights_in, 16)
            step(0, 0, first=True)
            sp.wait_ge(sign_ready, 2)
            load_adj(3, 1)
            sp.wait_ge(y_ready, 1)
            load_x(2, 0)
            sp.wait_ge(result_ready, 1)
            store(0, 0)
            with sp.Fori(1, PAIRS - 1) as j:
                with sp.If(j % PPG == PPG - 1):
                    sp.wait_ge(part_ready, PARTS * ((j + 1) // PPG))
                    load_split((j + 1) // PPG)
                step(j, 0)
                step(j, 1)
            step(PAIRS - 1, 0, last=True)
            step(PAIRS - 1, 1, last=True)
            sp.wait_ge(result_ready, TILES)
            store(TILES - 1, 1)
            for i in range(2):
                sp.wait_ge(stored[i], 16 * PAIRS)

        @block.gpsimd
        def _(pool):
            pool.memset(ident_b[:], 0.0).then_inc(const_pool, 1)
            pool.memset(ident_f[:], 0.0).then_inc(const_pool, 1)
            pool.memset(pack_tmp[:], 0.0).then_inc(const_pool, 1)
            pool.memset(ones_row[:], 1.0).then_inc(const_pool, 1)
            pool.memset(ones_col[:], 1.0).then_inc(const_pool, 1)
            pool.memset(ones_b[:], 1.0).then_inc(const_pool, 1)
            pool.memset(before_b[:], 1.0).then_inc(const_pool, 1)
            pool.memset(eps_col[:], EPS).then_inc(const_pool, 1)
            pool.iota(word_rank[:], pattern=[[-256, NW]], base=256 * NW, channel_multiplier=0,
                      allow_small_or_imprecise_dtypes=True).then_inc(const_pool, 1)
            pool.iota(behind[:], pattern=[[0, WORDS_KEPT], [-1, WORD]], base=WORD, channel_multiplier=0,
                      allow_small_or_imprecise_dtypes=True).then_inc(const_pool, 1)
            pool.iota(row_base[:].rearrange("p (b h) -> p b h", b=B), pattern=[[N, B], [0, PPG]],
                      base=OFF, channel_multiplier=0,
                      allow_small_or_imprecise_dtypes=True).then_inc(const_pool, 1)
            for c in range(WORD):
                pool.memset(bit_of[:, :, c], 1 << (WORD - 1 - c)).then_inc(const_pool, 1)
            for q in range(LOW):
                pool.memset(edge[:, q:q + 1], float(OFF - WINDOW[q] * P)).then_inc(const_pool, 1)
            pool.wait_ge(const_pool, CONST_FILLS)
            for m in (ident_b, ident_f):
                pool.affine_select(out=m[:], in_=m[:], compare_op=ALU.not_equal, fill=1.0, base=0,
                                   pattern=[[-1, P]], channel_multiplier=1).then_inc(const_pool, 1)
            pool.affine_select(out=before_b[:], in_=before_b[:], compare_op=ALU.is_gt, fill=0.0, base=0,
                               pattern=[[1, P]], channel_multiplier=-1).then_inc(const_pool, 1)
            for c in range(WORD):
                pool.affine_select(out=pack_tmp[:, :, c], in_=pack_tmp[:, :, c], compare_op=ALU.not_equal,
                                   fill=float(1 << (WORD - 1 - c)), base=-c, pattern=[[-WORD, WPC]],
                                   channel_multiplier=1).then_inc(const_pool, 1)
            pool.wait_ge(const_pool, CONST_POOL - 1)
            pool.affine_select(out=before_b[:], in_=before_b[:], compare_op=ALU.not_equal, fill=SELF, base=0,
                               pattern=[[-1, P]], channel_multiplier=1).then_inc(const_pool, 1)

            def gather(out, at, done):
                pool.indirect_dma_start(
                    out=out, out_offset=None, in_=x_rows,
                    in_offset=bass.IndirectOffsetOnAxis(ap=at, axis=0)).then_inc(done, 16)

            def step(j, i, used_before=True, reduced_before=True):
                pool.wait_ge(index_ready, 2 * j + i + 1)
                if used_before:
                    pool.wait_ge(got_used, 2 * j + i - 1)
                pool.sem_inc(far_begun, 1)
                for s in range(FAR):
                    gather(got[:, i, s, :], index[:, i, s:s + 1], gathered[i][s >= EARLY])
                pool.wait_ge(flag_ready, 2 * j + i + 1)
                pool.sem_inc(flag_known, 1)
                overflow = pool.value_load(flag[0:1, i:i + 1])
                with pool.If(overflow != 0):
                    if reduced_before:
                        pool.wait_ge(agg_ready, 2 * j + i)
                    pool.sem_inc(low_begun, 1)
                    for q in range(LOW):
                        gather(got_low[:, q, :], index_low[:, i, q:q + 1], low_gathered)
                    pool.drain()
                pool.sem_inc(low_settled, 1)

            step(0, 0, used_before=False, reduced_before=False)
            step(0, 1, used_before=False)
            with pool.Fori(1, PAIRS) as j:
                step(j, 0)
                step(j, 1)

        @block.scalar
        def _(act):
            def make_mask(j, i):
                act.wait_ge(adj_in[i], 16 * (j + 1))
                act.activation(sign[:, i, :], adj_sb[:, i, :], ACT.Sign).then_inc(sign_ready, 1)

            def move_mask(j, i):
                act.wait_ge(turned, 2 * j + i + 1)
                act.activation(mask_t[:, i, :], turned_ps[:], ACT.Square).then_inc(mask_ready, 1)
                act.wait_ge(ranks_in_ps, 2 * j + i + 1)
                act.activation(rank[:, i, :], rank_ps[:, 0:WIN * P], ACT.Copy).then_inc(rank_ready, 1)

            def move_h(j, i):
                act.wait_ge(xt_ready, 2 * j + i + 1)
                act.activation(h_t[:, i, 0:C], turn_ps, ACT.Copy).then_inc(xt_moved, 1)
                act.wait_ge(at_ready, 2 * j + i + 1)
                act.activation(h_t[:, i, C:2 * C], turn_ps, ACT.Copy).then_inc(at_moved, 1)

            def finish(j, i, stored_before=True):
                act.wait_ge(stat_ready, 2 * j + i + 1)
                act.activation(std[:, i:i + 1], stat[:, i, 1:2], ACT.Sqrt, bias=eps_col[:]).then_inc(std_ready, 1)
                if stored_before:
                    act.wait_ge(stored[i], 16 * j)
                act.wait_ge(scale_ready, 2 * j + i + 1)
                act.activation(result[:, i, :], y[:, i, :], ACT.Identity, bias=shift[:, i:i + 1],
                               scale=rstd[:, i:i + 1]).then_inc(result_ready, 1)

            def make_part(g, n):
                if n == 0:
                    act.wait_ge(split_in, 16 * (g + 1))
                else:
                    act.wait_ge(rest_ready, (PARTS - 1) * g + n)
                act.activation(parts_next[:, :, n, :], x_rest[:], ACT.Copy).then_inc(part_ready, 1)

            def place_parts(g, t=None):
                act.wait_ge(part_ready, PARTS * (g + 1))
                if t is not None:
                    act.wait_ge(low_ready, t)
                act.activation(parts[:], parts_next[:], ACT.Copy).then_inc(parts_placed, 1)

            act.wait_ge(const_pool, CONST_FILLS)
            for i in range(2):
                make_mask(0, i)
                move_mask(0, i)
            for n in range(PARTS):
                make_part(0, n)
            place_parts(0)

            def step(j, i, first=False, last=False, stored_before=True):
                if not last:
                    make_mask(j + 1, i)
                if not first:
                    finish(j - 1 + i, 1 - i, stored_before)
                if not last:
                    move_mask(j + 1, i)
                move_h(j, i)

            step(0, 0, first=True)
            step(0, 1, stored_before=False)
            step(1, 0, stored_before=False)
            step(1, 1)
            with act.Fori(2, PAIRS - 1) as j:
                with act.If(j % PPG == 0):
                    place_parts(j // PPG, 2 * j)
                with act.If(j % PPG == PPG - 1):
                    make_part((j + 1) // PPG, 0)
                step(j, 0)
                with act.If(j % PPG == PPG - 1):
                    make_part((j + 1) // PPG, 1)
                step(j, 1)
                with act.If(j % PPG == PPG - 1):
                    make_part((j + 1) // PPG, 2)
            step(PAIRS - 1, 0, last=True)
            step(PAIRS - 1, 1, last=True)
            finish(PAIRS - 1, 1)

        @block.tensor
        def _(pe):
            def prepare(j, i, first=False):
                pe.wait_ge(sign_ready, 2 * j + i + 1)
                if not first:
                    pe.wait_ge(rank_ready, 2 * j + i)
                for c in range(CHUNKS):
                    mm = pe.transpose(turned_ps[:, c * P:(c + 1) * P], sign[:, i, c * P:(c + 1) * P], ident_b[:])
                mm.then_inc(turned, 1)
                pe.wait_ge(mask_ready, 2 * j + i + 1)
                for a in range(0, WIN, BANK // P):
                    b = min(a + BANK // P, WIN)
                    pe.matmul(rank_ps[:, a * P:b * P], before_b[:], mask_t[:, i, a * P:b * P],
                              start=True, stop=False, skip_group_check=True)
                    for c in range(b - 1):
                        to = max(a, c + 1)
                        mm = pe.matmul(rank_ps[:, to * P:b * P].rearrange("p (c r) -> p c r", r=P), ones_b[:],
                                       mask_t[:, i, None, c * P:(c + 1) * P].to_broadcast([P, b - to, P]),
                                       start=False, stop=(c == b - 2), skip_group_check=True)
                mm.then_inc(ranks_in_ps, 1)
                if not first:
                    pe.wait_ge(bits_used, 2 * j + i)
                for c in range(CHUNKS):
                    mm = pe.matmul(bits_ps[:, c * WPC:(c + 1) * WPC], mask_t[:, i, c * P:(c + 1) * P],
                                   pack[:], start=True, stop=True)
                mm.then_inc(bits_ready, 1)

            def fetch_low(j, i, g, first=False):
                pe.wait_ge(hot_ready, 2 * j + i + 1)
                pe.wait_ge(parts_placed, g + 1)
                if not first:
                    pe.wait_ge(agg_ready, 2 * j + i)
                for q in range(LOW):
                    for c in range(WINDOW[q]):
                        at = (HOT_AT[q] + c) * P
                        for n in range(PARTS):
                            mm = pe.matmul(low_ps[:, q, :], hot[:, i, at:at + P], parts[:, c, n, :],
                                           start=(c == 0 and n == 0), stop=(c == WINDOW[q] - 1 and n == PARTS - 1),
                                           skip_group_check=True)
                mm.then_inc(low_ready, 1)

            def sum_over(j, i):
                pe.wait_ge(over_ready, 2 * j + i + 1)
                pe.wait_ge(bits_used, 2 * j + i + 1)
                pe.matmul(flag_ps, ones_col[:], over[:], start=True, stop=True,
                          skip_group_check=True).then_inc(flag_in_ps, 1)

            def layer(j, i, first=False, ahead=2):
                pe.wait_ge(x_in[i], 16 * (j + 1))
                if not first:
                    pe.wait_ge(y_ready, 2 * j + i)
                pe.wait_ge(rank_ready, 2 * j + i + 1 + ahead)
                for c in range(CT):
                    mm = pe.transpose(turn_ps[:, c * P:(c + 1) * P], x_sb[:, i, c * P:(c + 1) * P], ident_f[:])
                mm.then_inc(xt_ready, 1)
                pe.wait_ge(xt_moved, 2 * j + i + 1)
                pe.matmul(layer_ps[:, 0:OUT], ones_row[:], b_row[:], start=True, stop=False)
                for k in range(CT):
                    pe.matmul(layer_ps[:, 0:OUT], h_t[:, i, k * P:(k + 1) * P], w_sb[:, k, :],
                              start=False, stop=False)
                pe.wait_ge(agg_ready, 2 * j + i + 1)
                for c in range(CT):
                    mm = pe.transpose(turn_ps[:, c * P:(c + 1) * P], agg[:, i, c * P:(c + 1) * P], ident_f[:])
                mm.then_inc(at_ready, 1)
                pe.wait_ge(at_moved, 2 * j + i + 1)
                for k in range(CT, KT):
                    mm = pe.matmul(layer_ps[:, 0:OUT], h_t[:, i, k * P:(k + 1) * P], w_sb[:, k, :],
                                   start=False, stop=(k == KT - 1))
                mm.then_inc(layer_ready, 1)

            pe.wait_ge(const_pool, CONST_POOL)
            pe.wait_ge(const_vec, 2)
            prepare(0, 0, first=True)
            prepare(0, 1)
            sum_over(0, 0)
            fetch_low(0, 0, 0, first=True)
            prepare(1, 0)
            sum_over(0, 1)
            pe.wait_ge(weights_in, 32)
            layer(0, 0, first=True)
            fetch_low(0, 1, 0)
            prepare(1, 1)
            sum_over(1, 0)
            layer(0, 1)
            with pe.Fori(1, PAIRS - 1) as j:
                fetch_low(j, 0, j // PPG)
                prepare(j + 1, 0)
                sum_over(j, 1)
                layer(j, 0)
                fetch_low(j, 1, j // PPG)
                prepare(j + 1, 1)
                sum_over(j + 1, 0)
                layer(j, 1)
            fetch_low(PAIRS - 1, 0, B - 1)
            sum_over(PAIRS - 1, 1)
            layer(PAIRS - 1, 0, ahead=1)
            fetch_low(PAIRS - 1, 1, B - 1)
            layer(PAIRS - 1, 1, ahead=0)

        @block.vector
        def _(dve):
            marks = [0]

            def mark(ins):
                ins.then_inc(vec, 1)
                marks[0] += 1
                return marks[0]

            def after(mark):
                dve.wait_ge(vec, mark)

            def restart():
                after(marks[0])
                dve.sem_clear(vec)
                marks[0] = 0

            def find(j, i, flag_before=True, done=None):
                dj, di = done or (None, None)

                def one_hot(q):
                    return dve.tensor_scalar(hot[:, i, HOT_AT[q] * P:(HOT_AT[q] + WINDOW[q]) * P],
                                             rank[:, i, 0:WINDOW[q] * P], SELF + q, None, ALU.is_equal)

                dve.wait_ge(bits_ready, 2 * j + i + 1)
                if flag_before:
                    dve.wait_ge(flag_in_ps, 2 * j + i)
                m = mark(dve.scalar_tensor_tensor(ranked[:], bits_ps[:, 0:NW], 0.0, word_rank[:], ALU.is_gt,
                                                  ALU.mult))
                if flag_before:
                    dve.tensor_reduce(flag[:, 1 - i:2 - i], flag_ps, AX.X, ALU.max).then_inc(flag_ready, 1)
                after(m)
                m = mark(dve.tensor_tensor(key[:], ranked[:], bits_ps[:, 0:NW], ALU.add))
                dve.engine_nop().then_inc(bits_used, 1)
                after(m)
                m = mark(dve.max(word_top[:, 0:8], key[:]))
                dve.wait_ge(rank_ready, 2 * j + i + 1)
                one_hot(0)
                after(m)
                m = mark(dve.match_replace(key[:], word_top[:, 0:8], key[:], 0.0))
                one_hot(1)
                after(m)
                m = mark(dve.max(word_top[:, 8:16], key[:]))
                one_hot(2)
                after(m)
                m = mark(dve.match_replace(key[:], word_top[:, 8:16], key[:], 0.0))
                one_hot(3)
                after(m)
                m = mark(dve.max(word_top[:, 16:24], key[:]))
                one_hot(4)
                after(m)
                m = mark(dve.match_replace(key[:], word_top[:, 16:24], key[:], 0.0))
                one_hot(5).then_inc(hot_ready, 1)
                after(m)
                m = mark(dve.max(word_top[:, 24:32], key[:]))
                after(m)
                m = mark(dve.tensor_copy(word_int[:], word_top[:, 0:WORDS_KEPT]))
                after(m)
                m = mark(dve.tensor_scalar(word_at[:], word_int[:], 8, 3, ALU.logical_shift_right,
                                           ALU.logical_shift_left))
                dve.tensor_tensor(bits_on[:], word_int[:, :, None].to_broadcast([P, WORDS_KEPT, WORD]),
                                  bit_of[:], ALU.bitwise_and)
                after(m)
                m = mark(dve.tensor_tensor(score[:], word_at[:, :, None].to_broadcast([P, WORDS_KEPT, WORD]),
                                           behind[:], ALU.add))
                after(m)
                m = mark(dve.scalar_tensor_tensor(cand[:], bits_on[:].rearrange("p a b -> p (a b)"), 0.0,
                                                  score[:].rearrange("p a b -> p (a b)"), ALU.is_gt, ALU.mult))
                for r in range(0, TOP, 8):
                    within = cand[:, 0:min((r + 8) * WORD, CAND)]
                    after(m)
                    m = mark(dve.max(top[:, r:r + 8], within))
                    if done and r == 8:
                        dve.wait_ge(layer_ready, 2 * dj + di + 1)
                        dve.scalar_tensor_tensor(y[:, di, :], layer_ps[:, 0:OUT], 0.0, x_sb[:, di, :], ALU.max,
                                                 ALU.add).then_inc(y_ready, 1)
                    if done and r == 16:
                        after(n)
                        dve.bn_aggr(stat[:, di, :], halves[:]).then_inc(stat_ready, 1)
                    if r + 8 < TOP:
                        after(m)
                        m = mark(dve.match_replace(within, top[:, r:r + 8], within, 0.0))
                        if done and r == 8:
                            dve.wait_ge(y_ready, 2 * dj + di + 1)
                            n = mark(dve.bn_stats(halves[:], y[:, di, :]))
                n = mark(dve.tensor_scalar_max(first[:], top[:, 0:1], float(WORD + 1)))
                m = mark(dve.tensor_tensor(outside[:], top[:, 0:LOW], edge[:], ALU.is_le))
                after(n)
                n = mark(dve.tensor_scalar(empty_low[:], top[:, 0:LOW], 0.0, first[:], ALU.is_equal, ALU.mult))
                dve.tensor_copy(spare[:, 0:FAR - LOW], first[:].to_broadcast([P, FAR - LOW]))
                after(n)
                n = mark(dve.tensor_tensor(spare[:, FAR - 1:FAR - 1 - LOW:-1], empty_low[:], top[:, 0:LOW],
                                           ALU.add))
                after(m)
                dve.tensor_tensor(over[:], outside[:], top[:, S - 1:S - 1 - LOW:-1],
                                  ALU.mult).then_inc(over_ready, 1)
                after(n)
                n = mark(dve.scalar_tensor_tensor(fill[:], top[:, LOW:S], 0.0, spare[:], ALU.is_equal, ALU.mult))
                base = row_base[:, bass.ds(j, 1)]
                dve.tensor_scalar(index_low[:, i, :], spare[:, FAR - LOW:FAR], -1.0, base, ALU.mult, ALU.add)
                after(n)
                n = mark(dve.tensor_tensor(chosen[:], fill[:], top[:, LOW:S], ALU.add))
                dve.tensor_scalar(low[:, i:i + 1], top[:, S:S + 1], 0.0, -BIG, ALU.is_gt, ALU.mult)
                after(n)
                dve.tensor_scalar(index[:, i, :], chosen[:], -1.0, base, ALU.mult, ALU.add).then_inc(index_ready, 1)
                if done:
                    dve.wait_ge(std_ready, 2 * dj + di + 1)
                    n = mark(dve.reciprocal(rstd[:, di:di + 1], std[:, di:di + 1]))
                dve.tensor_scalar(high[:, i:i + 1], top[:, 0:1], 0.0, BIG, ALU.is_gt, ALU.mult)
                if done:
                    after(n)
                    dve.scalar_tensor_tensor(shift[:, di:di + 1], stat[:, di, 0:1], -1.0, rstd[:, di:di + 1],
                                             ALU.mult, ALU.mult).then_inc(scale_ready, 1)

            def reduce(j, i):
                dve.wait_ge(flag_ready, 2 * j + i + 1)
                dve.sem_inc(flag_seen, 1)
                overflow = dve.value_load(flag[0:1, i:i + 1])

                def most(a, b, into):
                    return dve.tensor_reduce(into, got[:, i, a:b, :].rearrange("p k c -> p c k"), AX.X, ALU.max)

                dve.wait_ge(gathered[i][0], 16 * EARLY * (j + 1))
                most(0, EARLY, got[:, i, FAR, :])
                with dve.If(overflow != 0):
                    dve.wait_ge(low_settled, 2 * j + i + 1)
                    dve.wait_ge(low_ready, 2 * j + i + 1)
                    dve.tensor_reduce(got[:, i, FAR + 1, :], got_low[:].rearrange("p q c -> p c q"), AX.X, ALU.max)
                with dve.If(overflow == 0):
                    dve.wait_ge(low_ready, 2 * j + i + 1)
                    dve.tensor_reduce(got[:, i, FAR + 1, :], low_ps[:].rearrange("p q c -> p c q"), AX.X, ALU.max)
                m = mark(dve.engine_nop())
                after(m)
                dve.wait_ge(gathered[i][1], 16 * (FAR - EARLY) * (j + 1))
                most(EARLY, FAR + 2, all_max[:]).then_inc(got_used, 1)
                dve.wait_ge(got_used, 2 * j + i + 1)
                dve.tensor_scalar(agg[:, i, :], all_max[:], low[:, i:i + 1], high[:, i:i + 1],
                                  ALU.max, ALU.min).then_inc(agg_ready, 1)

            def finish(j, i):
                dve.wait_ge(layer_ready, 2 * j + i + 1)
                dve.scalar_tensor_tensor(y[:, i, :], layer_ps[:, 0:OUT], 0.0, x_sb[:, i, :], ALU.max,
                                         ALU.add).then_inc(y_ready, 1)
                dve.wait_ge(y_ready, 2 * j + i + 1)
                after(mark(dve.bn_stats(halves[:], y[:, i, :])))
                dve.bn_aggr(stat[:, i, :], halves[:]).then_inc(stat_ready, 1)
                dve.wait_ge(std_ready, 2 * j + i + 1)
                after(mark(dve.reciprocal(rstd[:, i:i + 1], std[:, i:i + 1])))
                dve.scalar_tensor_tensor(shift[:, i:i + 1], stat[:, i, 0:1], -1.0, rstd[:, i:i + 1],
                                         ALU.mult, ALU.mult).then_inc(scale_ready, 1)

            def take_off(g, n):
                dve.wait_ge(part_ready, PARTS * g + n + 1)
                dve.tensor_tensor(x_rest[:], x_rest[:], parts_next[:, :, n, :], ALU.subtract).then_inc(rest_ready, 1)

            dve.wait_ge(const_pool, CONST_POOL)
            dve.tensor_reduce(pack_f[:], pack_tmp[:], AX.X, ALU.add).then_inc(const_vec, 1)
            dve.wait_ge(const_vec, 1)
            dve.tensor_copy(pack[:], pack_f[:]).then_inc(const_vec, 1)

            find(0, 0, flag_before=False)
            take_off(0, 0)
            take_off(0, 1)
            find(0, 1)
            reduce(0, 0)
            find(1, 0, done=(0, 0))
            reduce(0, 1)
            restart()
            with dve.Fori(1, PAIRS - 1) as j:
                find(j, 1, done=(j - 1, 1))
                with dve.If(j % PPG == PPG - 1):
                    take_off((j + 1) // PPG, 0)
                reduce(j, 0)
                find(j + 1, 0, done=(j, 0))
                with dve.If(j % PPG == PPG - 1):
                    take_off((j + 1) // PPG, 1)
                reduce(j, 1)
                restart()
            find(PAIRS - 1, 1, done=(PAIRS - 2, 1))
            reduce(PAIRS - 1, 0)
            dve.wait_ge(flag_in_ps, TILES)
            dve.tensor_reduce(flag[:, 1:2], flag_ps, AX.X, ALU.max).then_inc(flag_ready, 1)
            finish(PAIRS - 1, 0)
            reduce(PAIRS - 1, 1)
            finish(PAIRS - 1, 1)


_INS = ["x", "adj", "L0_gnn_W", "L0_gnn_b"]


def kernel(**inputs):
    import numpy as np
    import concourse.bacc as bacc
    from concourse.bass_utils import run_bass_kernel_spmd

    nc = bacc.Bacc("TRN2", target_bir_lowering=False, num_devices=1)
    arrays, args = {}, []
    for name in _INS:
        a = np.ascontiguousarray(inputs[name])
        arrays[f"in_{name}"] = a
        args.append(nc.dram_tensor(f"in_{name}", a.shape, mybir.dt.from_np(a.dtype), kind="ExternalInput").ap())
    out = nc.dram_tensor("out", inputs["x"].shape, F32, kind="ExternalOutput").ap()
    build(nc, *args, out)
    return run_bass_kernel_spmd(nc, [arrays], core_ids=[0]).results[0]["out"]
```

```python
from contextlib import ExitStack

import concourse.bass as bass
from concourse import mybir

P = 128
S = 25
WINDOW = (2, 3, 4, 5, 5, 6, 6, 6)
LOW = len(WINDOW)
LOW_A = 5
FAR = S - LOW
WORD = 8
TOP = 32
WORDS_KEPT = S + 1
CAND = WORDS_KEPT * WORD
SELF = 1024.0
PARTS = 3
BANK = 512
EPS = 1e-5
SHARE = 8
BIG = 3.4028234663852886e38

ALU = mybir.AluOpType
ACT = mybir.ActivationFunctionType
AX = mybir.AxisListType
BF16 = mybir.dt.bfloat16
F16 = mybir.dt.float16
F32 = mybir.dt.float32
I32 = mybir.dt.int32


def build(nc, x, adj, w, bias, out):
    B, N, C = x.shape
    OUT = w.shape[1]
    TILES = B * N // P
    PAIRS = TILES // 2
    PER_GRAPH = N // P
    PPG = PER_GRAPH // 2
    CHUNKS = N // P
    NW = N // WORD
    WPC = P // WORD
    CT = C // P
    KT = w.shape[0] // P
    WIN = max(WINDOW)
    HOTS = sum(WINDOW)
    HOT_AT = [sum(WINDOW[:q]) for q in range(LOW)]
    OFF = N + WORD
    assert TILES % 2 == 0 and PER_GRAPH % 2 == 0 and KT == 2 * CT
    assert LOW == 8 and 2 * LOW <= S
    assert CT == 2 and LOW_A <= LOW - 2 and LOW % 2 == 0
    assert 1 < WIN and WIN * P < SELF and 2 * WIN * P <= N and N <= 2 * SELF

    x_rows = x.rearrange("b n c -> (b n) c")
    x_tiles = x.rearrange("b (t p) c -> (b t) p c", p=P)
    x_heads = x[:, 0:WIN * P, :].rearrange("b (c p) f -> b p c f", p=P)
    adj_tiles = adj.rearrange("b (t p) m -> (b t) p m", p=P)
    out_tiles = out.rearrange("b (t p) c -> (b t) p c", p=P)

    with ExitStack() as ctx:
        def sb(name, shape, dt):
            return ctx.enter_context(nc.sbuf_tensor(name, shape, dt))

        def ps(name, shape, dt):
            return ctx.enter_context(nc.psum_tensor(name, shape, dt))

        def sem(name):
            return ctx.enter_context(nc.semaphore(name))

        ident_b = sb("ident_b", [P, P], BF16)
        ident_f = sb("ident_f", [P, P], F32)
        ones_b = sb("ones_b", [P, P], BF16)
        before_b = sb("before_b", [P, P], BF16)
        pack_f = sb("pack_f", [P, WPC], F32)
        pack_tmp = sb("pack_tmp", [P, WPC, WORD], F32)
        pack = sb("pack", [P, WPC], BF16)
        word_rank = sb("word_rank", [1, 2, NW], BF16)
        one_b = sb("one_b", [1, P], BF16)
        bit_of = sb("bit_of", [P, WORDS_KEPT, WORD], I32)
        behind = sb("behind", [P, WORDS_KEPT, WORD], F32)
        row_base = sb("row_base", [P, PAIRS], F32)
        edge = sb("edge", [P, LOW], F32)
        ones_row = sb("ones_row", [1, P], F32)
        ones_col = sb("ones_col", [P, 1], F32)
        w_sb = sb("w_sb", [P, KT, OUT], F32)
        b_row = sb("b_row", [1, OUT], F32)
        eps_col = sb("eps_col", [P, 1], F32)

        adj_sb = sb("adj_sb", [P, 2, N], I32)
        x_sb = sb("x_sb", [P, 2, C], F32)
        sign = sb("sign", [P, 2, N], BF16)
        mask_t = sb("mask_t", [P, 2, N], BF16)
        rank = sb("rank", [P, 2, WIN * P], F16)
        hot = sb("hot", [P, 2, HOTS * P], BF16)
        got = sb("got", [P, 2, FAR + 1, C], F32)
        index = sb("index", [P, 2, FAR], I32)
        index_low = sb("index_low", [P, 2, LOW], I32)
        flag = sb("flag", [1, 2], I32)
        low = sb("low", [P, 2], F32)
        high = sb("high", [P, 2], F32)
        agg = sb("agg", [P, 2, C], F32)
        h_t = sb("h_t", [P, 2, KT * P], F32)
        y = sb("y", [P, 2, OUT], F32)
        total = sb("total", [P, 2], F32)
        minus_mean = sb("minus_mean", [P, 2], F32)
        squares = sb("squares", [P, OUT], F32)
        spread = sb("spread", [P, 2], F32)
        std = sb("std", [P, 2], F32)
        rstd = sb("rstd", [P, 2], F32)
        shift = sb("shift", [P, 2], F32)
        result = sb("result", [P, 2, OUT], F32)

        got_low = sb("got_low", [P, LOW, C], F32)
        x_rest = sb("x_rest", [P, WIN, C], F32)
        parts_next = sb("parts_next", [P, WIN, PARTS, C], BF16)
        parts = sb("parts", [P, WIN, PARTS, C], BF16)

        numbered = sb("numbered", [P, NW], F32)
        key = sb("key", [P, NW], F32)
        word_top = sb("word_top", [P, TOP], F32)
        word_int = sb("word_int", [P, WORDS_KEPT], I32)
        word_at = sb("word_at", [P, WORDS_KEPT], I32)
        bits_on = sb("bits_on", [P, WORDS_KEPT, WORD], I32)
        score = sb("score", [P, WORDS_KEPT, WORD], F32)
        cand = sb("cand", [P, CAND], F32)
        top = sb("top", [P, TOP], F32)
        first = sb("first", [P, 1], F32)
        spare = sb("spare", [P, FAR], F32)
        empty_low = sb("empty_low", [P, LOW], F32)
        fill = sb("fill", [P, FAR], F32)
        chosen = sb("chosen", [P, FAR], F32)
        outside = sb("outside", [P, LOW], F32)
        over = sb("over", [P, LOW], F32)
        all_max = sb("all_max", [P, C], F32)

        turned_ps = ps("turned_ps", [P, N], BF16)
        rank_ps = turned_ps[:].bitcast(F32)
        flag_ps = rank_ps[0:1, WIN * P:WIN * P + LOW]
        bits_ps = ps("bits_ps", [P, 2, NW], F32)
        low_ps = ps("low_ps", [P, LOW, C], F32)
        at_ps = low_ps[:, LOW - 1, :]
        xt_ps = low_ps[:, LOW - 2, :]
        layer_ps = ps("layer_ps", [P, BANK], F32)

        const_pool = sem("const_pool")
        const_vec = sem("const_vec")
        weights_in = sem("weights_in")
        adj_in = [sem(f"adj_in{i}") for i in range(2)]
        x_in = [sem(f"x_in{i}") for i in range(2)]
        sign_ready = sem("sign_ready")
        turned = sem("turned")
        mask_ready = sem("mask_ready")
        ranks_in_ps = sem("ranks_in_ps")
        rank_ready = sem("rank_ready")
        bits_ready = sem("bits_ready")
        numbered_ready = sem("numbered_ready")
        bits_used = sem("bits_used")
        hot_ready = sem("hot_ready")
        index_ready = sem("index_ready")
        over_ready = sem("over_ready")
        flag_in_ps = sem("flag_in_ps")
        flag_ready = sem("flag_ready")
        far_begun = sem("far_begun")
        low_begun = sem("low_begun")
        flag_known = sem("flag_known")
        flag_seen = sem("flag_seen")
        gathered = [sem(f"gathered{i}") for i in range(2)]
        low_gathered = sem("low_gathered")
        low_settled = sem("low_settled")
        got_used = sem("got_used")
        low_ready = sem("low_ready")
        low_used = sem("low_used")
        agg_ready = sem("agg_ready")
        xt_ready = sem("xt_ready")
        xt_moved = sem("xt_moved")
        at_ready = sem("at_ready")
        at_moved = sem("at_moved")
        layer_ready = sem("layer_ready")
        y_ready = sem("y_ready")
        mean_ready = sem("mean_ready")
        spread_ready = sem("spread_ready")
        std_ready = sem("std_ready")
        rstd_ready = sem("rstd_ready")
        shift_ready = sem("shift_ready")
        result_ready = sem("result_ready")
        stored = [sem(f"stored{i}") for i in range(2)]
        split_in = sem("split_in")
        part_ready = sem("part_ready")
        rest_ready = sem("rest_ready")
        parts_placed = sem("parts_placed")
        vec = sem("vec")

        CONST_FILLS = 13 + WORD + LOW
        CONST_POOL = CONST_FILLS + 4 + WORD

        block = ctx.enter_context(nc.Block())

        @block.sync
        def _(sp):
            def load_adj(t, i):
                sp.dma_start(adj_sb[:, i, :], adj_tiles[t]).then_inc(adj_in[i], 16)

            def load_x(t, i):
                sp.dma_start(x_sb[:, i, :], x_tiles[t]).then_inc(x_in[i], 16)

            def load_split(g):
                sp.dma_start(x_rest[:], x_heads[g]).then_inc(split_in, 16)

            def store(t, i):
                sp.dma_start(out_tiles[t], result[:, i, :]).then_inc(stored[i], 16)

            def step(j, i, adj=True, features=True):
                if adj:
                    sp.wait_ge(sign_ready, 2 * j + i + 2)
                    load_adj(2 * j + (i + 3), 1 - i)
                if features:
                    sp.wait_ge(y_ready, 2 * j + i)
                    load_x(2 * j + (i + 1), 1 - i)
                sp.wait_ge(result_ready, 2 * j + i)
                store(2 * j + (i - 1), 1 - i)

            load_adj(0, 0)
            load_adj(1, 1)
            load_split(0)
            load_x(0, 0)
            load_x(1, 1)
            sp.dma_start(w_sb[:], w.rearrange("(k p) o -> p k o", p=P)).then_inc(weights_in, 16)
            sp.dma_start(b_row[:], bias.rearrange("(a o) -> a o", a=1)).then_inc(weights_in, 16)
            for i in range(2):
                sp.wait_ge(sign_ready, i + 1)
                load_adj(2 + i, i)
            sp.wait_ge(sign_ready, 3)
            load_adj(4, 0)
            sp.wait_ge(y_ready, 1)
            load_x(2, 0)
            sp.wait_ge(result_ready, 1)
            store(0, 0)
            with sp.Fori(1, PAIRS - 2) as j:
                with sp.If(j % PPG == PPG - 2):
                    sp.wait_ge(part_ready, PARTS * ((j + 2) // PPG))
                    load_split((j + 2) // PPG)
                step(j, 0)
                step(j, 1)
            step(PAIRS - 2, 0)
            step(PAIRS - 2, 1, adj=False)
            step(PAIRS - 1, 0, adj=False)
            step(PAIRS - 1, 1, adj=False, features=False)
            sp.wait_ge(result_ready, TILES)
            store(TILES - 1, 1)
            for i in range(2):
                sp.wait_ge(stored[i], 16 * PAIRS)

        @block.gpsimd
        def _(pool):
            pool.memset(ident_b[:], 0.0).then_inc(const_pool, 1)
            pool.memset(ident_f[:], 0.0).then_inc(const_pool, 1)
            pool.memset(pack_tmp[:], 0.0).then_inc(const_pool, 1)
            pool.memset(ones_row[:], 1.0).then_inc(const_pool, 1)
            pool.memset(ones_col[:], 1.0).then_inc(const_pool, 1)
            pool.memset(ones_b[:], 1.0).then_inc(const_pool, 1)
            pool.memset(before_b[:], 1.0).then_inc(const_pool, 1)
            pool.memset(eps_col[:], EPS).then_inc(const_pool, 1)
            pool.memset(one_b[:], 1.0).then_inc(const_pool, 1)
            pool.memset(word_rank[:, 0, :], 0.0).then_inc(const_pool, 1)
            pool.iota(word_rank[:, 1, :], pattern=[[-256, NW]], base=256 * NW, channel_multiplier=0,
                      allow_small_or_imprecise_dtypes=True).then_inc(const_pool, 1)
            pool.iota(behind[:], pattern=[[0, WORDS_KEPT], [-1, WORD]], base=WORD, channel_multiplier=0,
                      allow_small_or_imprecise_dtypes=True).then_inc(const_pool, 1)
            pool.iota(row_base[:].rearrange("p (b h) -> p b h", b=B), pattern=[[N, B], [0, PPG]],
                      base=OFF, channel_multiplier=0,
                      allow_small_or_imprecise_dtypes=True).then_inc(const_pool, 1)
            for c in range(WORD):
                pool.memset(bit_of[:, :, c], 1 << (WORD - 1 - c)).then_inc(const_pool, 1)
            for q in range(LOW):
                pool.memset(edge[:, q:q + 1], float(OFF - WINDOW[q] * P)).then_inc(const_pool, 1)
            pool.wait_ge(const_pool, CONST_FILLS)
            for m in (ident_b, ident_f):
                pool.affine_select(out=m[:], in_=m[:], compare_op=ALU.not_equal, fill=1.0, base=0,
                                   pattern=[[-1, P]], channel_multiplier=1).then_inc(const_pool, 1)
            pool.affine_select(out=before_b[:], in_=before_b[:], compare_op=ALU.is_gt, fill=0.0, base=0,
                               pattern=[[1, P]], channel_multiplier=-1).then_inc(const_pool, 1)
            for c in range(WORD):
                pool.affine_select(out=pack_tmp[:, :, c], in_=pack_tmp[:, :, c], compare_op=ALU.not_equal,
                                   fill=float(1 << (WORD - 1 - c)), base=-c, pattern=[[-WORD, WPC]],
                                   channel_multiplier=1).then_inc(const_pool, 1)
            pool.wait_ge(const_pool, CONST_POOL - 1)
            pool.affine_select(out=before_b[:], in_=before_b[:], compare_op=ALU.not_equal, fill=SELF, base=0,
                               pattern=[[-1, P]], channel_multiplier=1).then_inc(const_pool, 1)

            def gather(out, at, done):
                pool.indirect_dma_start(
                    out=out, out_offset=None, in_=x_rows,
                    in_offset=bass.IndirectOffsetOnAxis(ap=at, axis=0)).then_inc(done, 16)

            def step(j, i, used_before=True, reduced_before=True):
                pool.wait_ge(index_ready, 2 * j + i + 1)
                if used_before:
                    pool.wait_ge(got_used, 2 * j + i - 1)
                pool.sem_inc(far_begun, 1)
                for s in range(FAR):
                    gather(got[:, i, s, :], index[:, i, s:s + 1], gathered[i])
                pool.wait_ge(flag_ready, 2 * j + i + 1)
                pool.sem_inc(flag_known, 1)
                overflow = pool.value_load(flag[0:1, i:i + 1])
                with pool.If(overflow != 0):
                    if reduced_before:
                        pool.wait_ge(agg_ready, 2 * j + i)
                    pool.sem_inc(low_begun, 1)
                    for q in range(LOW):
                        gather(got_low[:, q, :], index_low[:, i, q:q + 1], low_gathered)
                    pool.drain()
                pool.sem_inc(low_settled, 1)

            step(0, 0, used_before=False, reduced_before=False)
            step(0, 1, used_before=False)
            with pool.Fori(1, PAIRS) as j:
                step(j, 0)
                step(j, 1)

        @block.scalar
        def _(act):
            def make_mask(j, i):
                act.wait_ge(adj_in[i], 16 * (j + 1))
                act.activation(sign[:, i, :], adj_sb[:, i, :], ACT.Sign).then_inc(sign_ready, 1)

            def move_mask(j, i):
                act.wait_ge(turned, 2 * j + i + 1)
                act.activation(mask_t[:, i, :], turned_ps[:], ACT.Square).then_inc(mask_ready, 1)

            def move_rank(j, i):
                act.wait_ge(ranks_in_ps, 2 * j + i + 1)
                act.activation(rank[:, i, :], rank_ps[:, 0:WIN * P], ACT.Copy).then_inc(rank_ready, 1)

            def move_numbered(j, i):
                act.wait_ge(bits_ready, 2 * j + i + 1)
                act.activation(numbered[:], bits_ps[:, 1, :], ACT.Copy).then_inc(numbered_ready, 1)

            def move_x(j, i):
                act.wait_ge(xt_ready, 2 * j + i + 1)
                act.activation(h_t[:, i, 0:C], xt_ps, ACT.Copy).then_inc(xt_moved, 1)

            def move_agg(j, i):
                act.wait_ge(at_ready, 2 * j + i + 1)
                act.activation(h_t[:, i, C:2 * C], at_ps, ACT.Copy).then_inc(at_moved, 1)

            def finish(j, i, stored_before=True):
                at = slice(i, i + 1)
                act.wait_ge(y_ready, 2 * j + i + 1)
                act.activation(minus_mean[:, at], total[:, at], ACT.Copy, scale=-1.0 / OUT).then_inc(mean_ready, 1)
                act.wait_ge(mean_ready, 2 * j + i + 1)
                act.activation(squares[:], y[:, i, :], ACT.Square, bias=minus_mean[:, at],
                               accum_out=spread[:, at]).then_inc(spread_ready, 1)
                act.wait_ge(spread_ready, 2 * j + i + 1)
                act.activation(std[:, at], spread[:, at], ACT.Sqrt, bias=eps_col[:],
                               scale=1.0 / OUT).then_inc(std_ready, 1)
                act.wait_ge(rstd_ready, 2 * j + i + 1)
                act.activation(shift[:, at], minus_mean[:, at], ACT.Copy, scale=rstd[:, at]).then_inc(shift_ready, 1)
                if stored_before:
                    act.wait_ge(stored[i], 16 * j)
                act.wait_ge(shift_ready, 2 * j + i + 1)
                act.activation(result[:, i, :], y[:, i, :], ACT.Identity, bias=shift[:, at],
                               scale=rstd[:, at]).then_inc(result_ready, 1)

            def make_part(g, n, placed_before=True):
                if n == 0:
                    act.wait_ge(split_in, 16 * (g + 1))
                    if placed_before:
                        act.wait_ge(parts_placed, g)
                else:
                    act.wait_ge(rest_ready, (PARTS - 1) * g + n)
                act.activation(parts_next[:, :, n, :], x_rest[:], ACT.Copy).then_inc(part_ready, 1)

            act.wait_ge(const_pool, CONST_FILLS)
            for i in range(2):
                make_mask(0, i)
                move_mask(0, i)
                move_rank(0, i)
                move_numbered(0, i)
            make_mask(1, 0)
            for n in range(PARTS):
                make_part(0, n, placed_before=False)

            def step(j, i, first=False, last=False, stored_before=True, near=None):
                move_x(j, i)
                if not last:
                    move_mask(j + 1, i)
                if not first:
                    finish(j - 1 + i, 1 - i, stored_before)
                if not last:
                    move_rank(j + 1, i)
                if near is not None:
                    with act.If(near):
                        make_part((j + 2) // PPG, 1 + i)
                if not (last or i == 1 and isinstance(j, int) and j == PAIRS - 2):
                    make_mask(j + 1 + i, 1 - i)
                if not last:
                    move_numbered(j + 1, i)
                move_agg(j, i)

            step(0, 0, first=True)
            step(0, 1, stored_before=False)
            step(1, 0, stored_before=False)
            step(1, 1)
            with act.Fori(2, PAIRS - 2) as j:
                with act.If(j % PPG == PPG - 2):
                    make_part((j + 2) // PPG, 0)
                step(j, 0, near=(j % PPG == PPG - 2))
                step(j, 1, near=(j % PPG == PPG - 2))
            step(PAIRS - 2, 0)
            step(PAIRS - 2, 1)
            step(PAIRS - 1, 0, last=True)
            step(PAIRS - 1, 1, last=True)
            finish(PAIRS - 1, 1)

        @block.tensor
        def _(pe):
            def turn_mask(j, i, chunks=range(CHUNKS), flag_before=True):
                if chunks[0] == 0:
                    pe.wait_ge(sign_ready, 2 * j + i + 1)
                    if flag_before:
                        pe.wait_ge(flag_ready, 2 * j + i - 1)
                for c in chunks:
                    mm = pe.transpose(turned_ps[:, c * P:(c + 1) * P], sign[:, i, c * P:(c + 1) * P], ident_b[:])
                if chunks[-1] == CHUNKS - 1:
                    mm.then_inc(turned, 1)

            def count(j, i, first=False):
                pe.wait_ge(mask_ready, 2 * j + i + 1)
                for a in range(0, WIN, BANK // P):
                    b = min(a + BANK // P, WIN)
                    pe.matmul(rank_ps[:, a * P:b * P], before_b[:], mask_t[:, i, a * P:b * P],
                              start=True, stop=False, skip_group_check=True)
                    for c in range(b - 1):
                        to = max(a, c + 1)
                        mm = pe.matmul(rank_ps[:, to * P:b * P].rearrange("p (c r) -> p c r", r=P), ones_b[:],
                                       mask_t[:, i, None, c * P:(c + 1) * P].to_broadcast([P, b - to, P]),
                                       start=False, stop=(c == b - 2), skip_group_check=True)
                mm.then_inc(ranks_in_ps, 1)
                if not first:
                    pe.wait_ge(bits_used, 2 * j + i)
                pe.matmul(bits_ps[:], one_b[:], word_rank[:], start=True, stop=False, skip_group_check=True)
                for c in range(CHUNKS):
                    mm = pe.matmul(bits_ps[:, :, c * WPC:(c + 1) * WPC], mask_t[:, i, c * P:(c + 1) * P],
                                   pack[:, None, :].to_broadcast([P, 2, WPC]), start=False, stop=(c == CHUNKS - 1),
                                   skip_group_check=True)
                mm.then_inc(bits_ready, 1)

            def turn_x(j, i):
                pe.wait_ge(x_in[i], 16 * (j + 1))
                for c in range(CT):
                    mm = pe.transpose(xt_ps[:, c * P:(c + 1) * P], x_sb[:, i, c * P:(c + 1) * P], ident_f[:])
                mm.then_inc(xt_ready, 1)

            def fetch(i, q):
                for c in range(WINDOW[q]):
                    at = (HOT_AT[q] + c) * P
                    for n in range(PARTS):
                        mm = pe.matmul(low_ps[:, q, :], hot[:, i, at:at + P], parts[:, c, n, :],
                                       start=(c == 0 and n == 0), stop=(c == WINDOW[q] - 1 and n == PARTS - 1),
                                       skip_group_check=True)
                return mm

            def fetch_a(j, i, g, first=False):
                pe.wait_ge(hot_ready, 2 * j + i + 1)
                pe.wait_ge(parts_placed, g + 1)
                if not first:
                    pe.wait_ge(low_used, 2 * j + i)
                for q in range(LOW_A):
                    fetch(i, q)

            def fetch_b(j, i):
                for q in range(LOW_A, LOW):
                    if q == LOW - 2:
                        pe.wait_ge(xt_moved, 2 * j + i + 1)
                    mm = fetch(i, q)
                mm.then_inc(low_ready, 1)

            def sum_over(j, i, ranks=None):
                pe.wait_ge(over_ready, 2 * j + i + 1)
                if ranks is not None:
                    pe.wait_ge(rank_ready, ranks)
                pe.matmul(flag_ps, ones_col[:], over[:], start=True, stop=True,
                          skip_group_check=True).then_inc(flag_in_ps, 1)

            def layer_x(j, i, first=False):
                if not first:
                    pe.wait_ge(y_ready, 2 * j + i)
                pe.wait_ge(xt_moved, 2 * j + i + 1)
                pe.matmul(layer_ps[:, 0:OUT], ones_row[:], b_row[:], start=True, stop=False)
                for k in range(CT):
                    pe.matmul(layer_ps[:, 0:OUT], h_t[:, i, k * P:(k + 1) * P], w_sb[:, k, :],
                              start=False, stop=False)

            def layer_agg(j, i, mask=None):
                pe.wait_ge(agg_ready, 2 * j + i + 1)
                for c in range(CT):
                    mm = pe.transpose(at_ps[:, c * P:(c + 1) * P], agg[:, i, c * P:(c + 1) * P], ident_f[:])
                mm.then_inc(at_ready, 1)
                if mask:
                    mask(range(SHARE))
                pe.wait_ge(at_moved, 2 * j + i + 1)
                for k in range(CT, KT):
                    mm = pe.matmul(layer_ps[:, 0:OUT], h_t[:, i, k * P:(k + 1) * P], w_sb[:, k, :],
                                   start=False, stop=(k == KT - 1))
                mm.then_inc(layer_ready, 1)

            def step(j, i, g, first=False, last=False):
                fetch_b(j, i)
                if not last:
                    count(j + 1, i)
                layer_x(j, i, first)
                if not (last and i == 1):
                    sum_over(j + i, 1 - i, ranks=None if last else 2 * j + i + 3)
                    fetch_a(j + i, 1 - i, g)
                if last or isinstance(j, int) and j == PAIRS - 2 and i == 1:
                    layer_agg(j, i)
                else:
                    layer_agg(j, i, lambda chunks: turn_mask(j + 1 + i, 1 - i, chunks))
                    turn_mask(j + 1 + i, 1 - i, range(SHARE, CHUNKS))
                if not (last and i == 1):
                    turn_x(j + i, 1 - i)

            pe.wait_ge(const_pool, CONST_POOL)
            pe.wait_ge(const_vec, 2)
            turn_mask(0, 0, flag_before=False)
            count(0, 0, first=True)
            pe.wait_ge(rank_ready, 1)
            turn_mask(0, 1, flag_before=False)
            count(0, 1)
            sum_over(0, 0, ranks=2)
            fetch_a(0, 0, 0, first=True)
            pe.wait_ge(weights_in, 32)
            turn_mask(1, 0)
            turn_x(0, 0)
            step(0, 0, 0, first=True)
            step(0, 1, 0)
            with pe.Fori(1, PAIRS - 2) as j:
                step(j, 0, j // PPG)
                step(j, 1, (j + 1) // PPG)
            step(PAIRS - 2, 0, B - 1)
            step(PAIRS - 2, 1, B - 1)
            step(PAIRS - 1, 0, B - 1, last=True)
            step(PAIRS - 1, 1, B - 1, last=True)

        @block.vector
        def _(dve):
            marks = [0]

            def mark(ins):
                ins.then_inc(vec, 1)
                marks[0] += 1
                return marks[0]

            def after(mark):
                dve.wait_ge(vec, mark)

            def restart():
                after(marks[0])
                dve.sem_clear(vec)
                marks[0] = 0

            def find(j, i, flag_before=True, done=None):
                def one_hot(q):
                    return dve.tensor_scalar(hot[:, i, HOT_AT[q] * P:(HOT_AT[q] + WINDOW[q]) * P],
                                             rank[:, i, 0:WINDOW[q] * P], SELF + q, None, ALU.is_equal)

                dve.wait_ge(numbered_ready, 2 * j + i + 1)
                m = mark(dve.scalar_tensor_tensor(key[:], bits_ps[:, 0, :], 512.0 * NW, numbered[:], ALU.mult,
                                                  ALU.min))
                dve.engine_nop().then_inc(bits_used, 1)
                if flag_before:
                    dve.wait_ge(flag_in_ps, 2 * j + i)
                    dve.tensor_reduce(flag[:, 1 - i:2 - i], flag_ps, AX.X, ALU.max).then_inc(flag_ready, 1)
                after(m)
                m = mark(dve.max(word_top[:, 0:8], key[:]))
                dve.wait_ge(rank_ready, 2 * j + i + 1)
                one_hot(0)
                after(m)
                m = mark(dve.match_replace(key[:], word_top[:, 0:8], key[:], 0.0))
                one_hot(1)
                after(m)
                m = mark(dve.max(word_top[:, 8:16], key[:]))
                one_hot(2)
                after(m)
                m = mark(dve.match_replace(key[:], word_top[:, 8:16], key[:], 0.0))
                one_hot(3)
                after(m)
                m = mark(dve.max(word_top[:, 16:24], key[:]))
                one_hot(4)
                after(m)
                m = mark(dve.match_replace(key[:], word_top[:, 16:24], key[:], 0.0))
                one_hot(5)
                after(m)
                m = mark(dve.max(word_top[:, 24:32], key[:]))
                one_hot(6)
                after(m)
                m = mark(dve.tensor_copy(word_int[:], word_top[:, 0:WORDS_KEPT]))
                one_hot(7).then_inc(hot_ready, 1)
                if done:
                    residual(*done)
                after(m)
                m = mark(dve.tensor_scalar(word_at[:], word_int[:], 8, 3, ALU.logical_shift_right,
                                           ALU.logical_shift_left))
                dve.tensor_tensor(bits_on[:], word_int[:, :, None].to_broadcast([P, WORDS_KEPT, WORD]),
                                  bit_of[:], ALU.bitwise_and)
                after(m)
                m = mark(dve.tensor_tensor(score[:], word_at[:, :, None].to_broadcast([P, WORDS_KEPT, WORD]),
                                           behind[:], ALU.add))
                after(m)
                m = mark(dve.scalar_tensor_tensor(cand[:], bits_on[:].rearrange("p a b -> p (a b)"), 0.0,
                                                  score[:].rearrange("p a b -> p (a b)"), ALU.is_gt, ALU.mult))
                def first_of(r):
                    return mark(dve.max(top[:, r:r + 8], cand[:, 0:min((r + 8) * WORD, CAND)]))

                def strike(r):
                    within = cand[:, 0:min((r + 8) * WORD, CAND)]
                    return mark(dve.match_replace(within, top[:, r:r + 8], within, 0.0))

                base = row_base[:, bass.ds(j, 1)]
                after(m)
                m = first_of(0)
                after(m)
                m = strike(0)
                n = mark(dve.tensor_scalar_max(first[:], top[:, 0:1], float(WORD + 1)))
                after(m)
                m = first_of(8)
                dve.tensor_tensor(outside[:], top[:, 0:LOW], edge[:], ALU.is_le)
                after(m)
                m = strike(8)
                n = mark(dve.tensor_scalar(empty_low[:], top[:, 0:LOW], 0.0, first[:], ALU.is_equal, ALU.mult))
                after(m)
                m = first_of(16)
                dve.tensor_copy(spare[:, 0:FAR - LOW], first[:].to_broadcast([P, FAR - LOW]))
                after(m)
                m = strike(16)
                n = mark(dve.tensor_tensor(spare[:, FAR - LOW:FAR], empty_low[:], top[:, 0:LOW], ALU.add))
                after(m)
                m = first_of(24)
                after(n)
                dve.tensor_scalar(index_low[:, i, :], spare[:, FAR - LOW:FAR], -1.0, base, ALU.mult, ALU.add)
                after(m)
                n = mark(dve.scalar_tensor_tensor(fill[:], top[:, LOW:S], 0.0, spare[:], ALU.is_equal, ALU.mult))
                dve.tensor_tensor(over[:], outside[:], top[:, S - LOW:S], ALU.mult).then_inc(over_ready, 1)
                after(n)
                n = mark(dve.tensor_tensor(chosen[:], fill[:], top[:, LOW:S], ALU.add))
                dve.tensor_scalar(low[:, i:i + 1], top[:, S:S + 1], 0.0, -BIG, ALU.is_gt, ALU.mult)
                after(n)
                dve.tensor_scalar(index[:, i, :], chosen[:], -1.0, base, ALU.mult, ALU.add).then_inc(index_ready, 1)
                dve.tensor_scalar(high[:, i:i + 1], top[:, 0:1], 0.0, BIG, ALU.is_gt, ALU.mult)
                if done:
                    invert(*done)

            def reduce(j, i, near=None):
                dve.wait_ge(flag_ready, 2 * j + i + 1)
                dve.sem_inc(flag_seen, 1)
                overflow = dve.value_load(flag[0:1, i:i + 1])
                dve.wait_ge(low_ready, 2 * j + i + 1)
                dve.tensor_reduce(got[:, i, FAR, :], low_ps[:, 0:LOW, :].rearrange("p q c -> p c q"), AX.X,
                                  ALU.max).then_inc(low_used, 1)
                with dve.If(overflow != 0):
                    dve.wait_ge(low_settled, 2 * j + i + 1)
                    dve.wait_ge(low_used, 2 * j + i + 1)
                    dve.tensor_reduce(got[:, i, FAR, :], got_low[:].rearrange("p q c -> p c q"), AX.X, ALU.max)
                if near is not None:
                    with dve.If(near):
                        place_parts((j + 1) // PPG)
                after(mark(dve.engine_nop()))
                dve.wait_ge(gathered[i], 16 * FAR * (j + 1))
                dve.tensor_reduce(all_max[:], got[:, i, :, :].rearrange("p k c -> p c k"), AX.X,
                                  ALU.max).then_inc(got_used, 1)
                dve.wait_ge(got_used, 2 * j + i + 1)
                dve.tensor_scalar(agg[:, i, :], all_max[:], low[:, i:i + 1], high[:, i:i + 1],
                                  ALU.max, ALU.min).then_inc(agg_ready, 1)

            def residual(j, i):
                dve.wait_ge(layer_ready, 2 * j + i + 1)
                dve.scalar_tensor_tensor(y[:, i, :], layer_ps[:, 0:OUT], 0.0, x_sb[:, i, :], ALU.max, ALU.add,
                                         accum_out=total[:, i:i + 1]).then_inc(y_ready, 1)

            def invert(j, i):
                dve.wait_ge(std_ready, 2 * j + i + 1)
                dve.reciprocal(rstd[:, i:i + 1], std[:, i:i + 1]).then_inc(rstd_ready, 1)

            def take_off(g, n):
                dve.wait_ge(part_ready, PARTS * g + n + 1)
                dve.tensor_tensor(x_rest[:], x_rest[:], parts_next[:, :, n, :], ALU.subtract).then_inc(rest_ready, 1)

            def place_parts(g):
                dve.wait_ge(part_ready, PARTS * (g + 1))
                dve.tensor_copy(parts[:], parts_next[:]).then_inc(parts_placed, 1)

            dve.wait_ge(const_pool, CONST_POOL)
            dve.tensor_reduce(pack_f[:], pack_tmp[:], AX.X, ALU.add).then_inc(const_vec, 1)
            dve.wait_ge(const_vec, 1)
            dve.tensor_copy(pack[:], pack_f[:]).then_inc(const_vec, 1)

            find(0, 0, flag_before=False)
            take_off(0, 0)
            take_off(0, 1)
            place_parts(0)
            find(0, 1)
            reduce(0, 0)
            find(1, 0, done=(0, 0))
            reduce(0, 1)
            restart()
            with dve.Fori(1, PAIRS - 1) as j:
                near = (j % PPG == PPG - 2)
                find(j, 1, done=(j - 1, 1))
                with dve.If(near):
                    with dve.If(j < PAIRS - 2):
                        take_off((j + 2) // PPG, 0)
                reduce(j, 0)
                find(j + 1, 0, done=(j, 0))
                with dve.If(near):
                    with dve.If(j < PAIRS - 2):
                        take_off((j + 2) // PPG, 1)
                reduce(j, 1, near=(j % PPG == PPG - 1))
                restart()
            find(PAIRS - 1, 1, done=(PAIRS - 2, 1))
            reduce(PAIRS - 1, 0)
            dve.wait_ge(flag_in_ps, TILES)
            dve.tensor_reduce(flag[:, 1:2], flag_ps, AX.X, ALU.max).then_inc(flag_ready, 1)
            for i in range(2):
                if i == 1:
                    reduce(PAIRS - 1, 1)
                residual(PAIRS - 1, i)
                invert(PAIRS - 1, i)


_INS = ["x", "adj", "L0_gnn_W", "L0_gnn_b"]


def kernel(**inputs):
    import numpy as np
    import concourse.bacc as bacc
    from concourse.bass_utils import run_bass_kernel_spmd

    nc = bacc.Bacc("TRN2", target_bir_lowering=False, num_devices=1)
    arrays, args = {}, []
    for name in _INS:
        a = np.ascontiguousarray(inputs[name])
        arrays[f"in_{name}"] = a
        args.append(nc.dram_tensor(f"in_{name}", a.shape, mybir.dt.from_np(a.dtype), kind="ExternalInput").ap())
    out = nc.dram_tensor("out", inputs["x"].shape, F32, kind="ExternalOutput").ap()
    build(nc, *args, out)
    return run_bass_kernel_spmd(nc, [arrays], core_ids=[0]).results[0]["out"]
```
